# Optimizing a Trainium2 kernel written in Bass

```python
import numpy as np
import jax
import jax.numpy as jnp

def _softmax(x, axis=-1):
    return jax.nn.softmax(x, axis=axis)

def _gelu(x):
    return jax.nn.gelu(x, approximate=True)

def _silu(x):
    return jax.nn.silu(x)

def _sigmoid(x):
    return jax.nn.sigmoid(x)

def _layernorm(x, axis=-1, eps=1e-05):
    m = jnp.mean(x, axis=axis, keepdims=True)
    v = jnp.var(x, axis=axis, keepdims=True)
    return (x - m) / jnp.sqrt(v + eps)

def _scatter_add(tgt, idx, src, axis=0):
    return tgt.at[idx].add(src)

def _segment_sum(src, seg, n):
    return jax.ops.segment_sum(src, seg, n)
kernel_name = 'mk_adaln_ffn_d1_seqx_r2_156cc9'

def setup_inputs(seed: int=0):
    np.random.seed(seed)
    _w = jnp.asarray

    def _rec_inputs():
        import jax
        import jax.numpy as jnp
        _rk = jax.random.key(seed)
        x = -0.0003929 + 0.9999 * jax.random.normal(jax.random.fold_in(_rk, 1), (8, 512, 1024), jnp.float32)
        _lenS = 512 - jax.random.randint(jax.random.fold_in(_rk, 7), (8,), 0, max(1, 512 // 4) + 1, jnp.int32)
        _lenS2 = 512 - jax.random.randint(jax.random.fold_in(_rk, 8), (8,), 0, max(1, 512 // 4) + 1, jnp.int32)
        cond_1 = jax.random.uniform(jax.random.fold_in(_rk, 11), (8, 1), jnp.float32, 0.0, 1.37214)
        return (x, cond_1)
    x, cond_1 = _rec_inputs()

    def _L0_cond_setup():
        import jax, jax.numpy as jnp
        import numpy as np
        B, S, D_MODEL, NHEAD = (4, 1024, 1024, 16)
        HEAD_DIM = D_MODEL // NHEAD
        key = jax.random.key(seed)
        ks = jax.random.split(key, 6)
        scale = 1.0 / np.sqrt(D_MODEL)
        return {'hidden_states': jax.random.normal(ks[0], (B, S, D_MODEL), dtype=jnp.float32), 'attention_precision': jax.random.uniform(ks[1], (B, 1, 1), dtype=jnp.float32, minval=0.5, maxval=2.0), 'Wq': jax.random.normal(ks[2], (D_MODEL, D_MODEL), dtype=jnp.float32) * scale, 'Wk': jax.random.normal(ks[3], (D_MODEL, D_MODEL), dtype=jnp.float32) * scale, 'Wv': jax.random.normal(ks[4], (D_MODEL, D_MODEL), dtype=jnp.float32) * scale, 'Wo': jax.random.normal(ks[5], (D_MODEL, D_MODEL), dtype=jnp.float32) * scale}
    _L0_cond_all = _L0_cond_setup()
    _L0_cond_in = {k: v for k, v in _L0_cond_all.items() if k in ('Wq', 'Wk', 'Wv', 'Wo')}
    del _L0_cond_all

    def _L0_ffn_setup():
        import jax, jax.numpy as jnp
        import numpy as np
        EPS = 1e-05

        def _ternary_weight(w, eps=EPS):
            alpha = jnp.maximum(jnp.mean(jnp.abs(w)), eps)
            return jnp.clip(jnp.round(w / alpha), -1.0, 1.0) * alpha

        def _absmax_act(x, eps=EPS):
            scale = jnp.maximum(jnp.max(jnp.abs(x), axis=-1, keepdims=True), eps) / 127.0
            return jnp.clip(jnp.round(x / scale), -128.0, 127.0) * scale
        key = jax.random.key(seed)
        k1, k2, k3 = jax.random.split(key, 3)
        B, S, D_IN, D_OUT = (4, 4096, 1024, 1024)
        x = jax.random.normal(k1, (B, S, D_IN), dtype=jnp.float32)
        bound_w = 1.0 / np.sqrt(D_IN)
        weight = jax.random.uniform(k2, (D_OUT, D_IN), dtype=jnp.float32, minval=-bound_w, maxval=bound_w)
        bias = jax.random.uniform(k3, (D_OUT,), dtype=jnp.float32, minval=-bound_w, maxval=bound_w)
        return {'x': x, 'weight': weight, 'bias': bias}
    _L0_ffn_all = _L0_ffn_setup()
    _L0_ffn_in = {k: v for k, v in _L0_ffn_all.items() if k in ('weight', 'bias')}
    del _L0_ffn_all
    return {'x': x, 'cond_1': cond_1, 'L0_cond_Wq': _L0_cond_in['Wq'], 'L0_cond_Wk': _L0_cond_in['Wk'], 'L0_cond_Wv': _L0_cond_in['Wv'], 'L0_cond_Wo': _L0_cond_in['Wo'], 'L0_ffn_weight': _L0_ffn_in['weight'], 'L0_ffn_bias': _L0_ffn_in['bias']}

def reference(x, cond_1, L0_cond_Wq, L0_cond_Wk, L0_cond_Wv, L0_cond_Wo, L0_ffn_weight, L0_ffn_bias):
    import jax
    import jax.numpy as jnp

    def _L0_cond_ref(hidden_states, attention_precision, Wq, Wk, Wv, Wo):
        import jax, jax.numpy as jnp
        import numpy as np
        B, S, D_MODEL, NHEAD = (4, 1024, 1024, 16)
        HEAD_DIM = D_MODEL // NHEAD
        b, s, _ = hidden_states.shape

        def proj(x, W):
            y = jnp.einsum('bsd,ed->bse', x, W)
            return y.reshape(b, s, NHEAD, HEAD_DIM).transpose(0, 2, 1, 3)
        q = proj(hidden_states, Wq)
        k = proj(hidden_states, Wk)
        v = proj(hidden_states, Wv)
        beta = jnp.minimum(attention_precision, 4.0)[:, None]
        q = q * beta
        scores = jnp.einsum('bhqd,bhkd->bhqk', q, k) / np.sqrt(HEAD_DIM)
        causal = jnp.tril(jnp.ones((s, s), dtype=bool))
        scores = jnp.where(causal, scores, jnp.finfo(scores.dtype).min)
        attn = jax.nn.softmax(scores, axis=-1)
        out = jnp.einsum('bhqk,bhkd->bhqd', attn, v)
        out = out.transpose(0, 2, 1, 3).reshape(b, s, D_MODEL)
        return jnp.einsum('bsd,ed->bse', out, Wo)

    def _L0_ffn_ref(x, weight, bias):
        import jax, jax.numpy as jnp
        import numpy as np
        EPS = 1e-05

        def _ternary_weight(w, eps=EPS):
            alpha = jnp.maximum(jnp.mean(jnp.abs(w)), eps)
            return jnp.clip(jnp.round(w / alpha), -1.0, 1.0) * alpha

        def _absmax_act(x, eps=EPS):
            scale = jnp.maximum(jnp.max(jnp.abs(x), axis=-1, keepdims=True), eps) / 127.0
            return jnp.clip(jnp.round(x / scale), -128.0, 127.0) * scale
        q_w = _ternary_weight(weight).astype(x.dtype)
        q_x = _absmax_act(x)
        return jnp.einsum('bsi,oi->bso', q_x, q_w) + bias.astype(x.dtype)
    x = x + _L0_ffn_ref(_L0_cond_ref(x, cond_1[:, None, :], L0_cond_Wq, L0_cond_Wk, L0_cond_Wv, L0_cond_Wo), L0_ffn_weight, L0_ffn_bias)
    return x

_drawn_inputs = setup_inputs


def setup_inputs(seed=0):
    import zlib

    import numpy as np

    out = dict(_drawn_inputs(seed))
    spreads = {}
    factors = {'L0_ffn_bias': 3.095}
    for name, (base, spread) in spreads.items():
        noise = np.random.default_rng([zlib.crc32(name.encode()), seed]).standard_normal(out[name].shape)
        drawn = base * np.exp(spread * noise) if base else spread * noise
        out[name] = jnp.asarray(drawn.astype(out[name].dtype))
    for name, factor in factors.items():
        out[name] = (out[name] * factor).astype(out[name].dtype)
    return out
```

```python
import concourse.bass as bass
from concourse import mybir
from contextlib import ExitStack

F32 = mybir.dt.float32
F32R = mybir.dt.float32r
BF16 = mybir.dt.bfloat16
ALU = mybir.AluOpType
ACT = mybir.ActivationFunctionType
AX = mybir.AxisListType

P = 128
B, S, D = 8, 512, 1024
DH = 64
KT = D // P
HG = 4
NG = D // DH // HG
EG = HG * DH
NBLK = HG // 2
QT = S // P
UNITS = HG * QT
STEPS = NG * B
MASKED = -3.0e38
EPS = 1e-5
MAGIC = 12582912.0
TILES = B * S // P


class Timetable:

    SLOTS = 16

    def __init__(self):
        self.entries = []

    def add(self, time, emit, *args):
        self.entries.append((time, len(self.entries), emit, args))

    def run(self, eng):
        for _, _, emit, args in sorted(self.entries, key=lambda x: x[:2]):
            emit(eng, *args)


def wait(eng, sem, value):
    if isinstance(value, int) and value <= 0:
        return
    eng.wait_ge(sem, value)


def apart(eng, passed):
    eng.sem_inc(passed, 1)


def attention_phase(nc, xT, cond, wq, wk, wv, oT):
    with ExitStack() as ctx:
        def sb(name, shape, dt):
            return ctx.enter_context(nc.sbuf_tensor(name, shape, dt))

        def sem(name):
            return ctx.enter_context(nc.semaphore(name))

        w_hi = [sb(f"w{n}_hi", [P, KT, EG], F32R) for n in "qkv"]
        w_lo = [sb(f"w{n}_lo", [P, KT, EG], F32R) for n in "qkv"]
        w_raw = [sb(f"w{n}_raw", [P, KT, EG], F32) for n in "qkv"]
        x_raw = sb("x_raw", [P, KT, S], F32)
        x_hi = sb("x_hi", [P, KT, S], F32R)
        x_lo = sb("x_lo", [P, KT, S], F32R)
        q_st = sb("q_st", [P, HG, S], F32R)
        k_st = sb("k_st", [P, HG, S], F32R)
        k_sw = sb("k_sw", [P, HG, S], F32R)
        v_st = sb("v_st", [P, QT, HG, 2, DH], F32R)
        prob = sb("prob", [P, 4, S], F32)
        pt_hi = [sb(f"pt_hi{i}", [P, QT, S], F32R) for i in range(2)]
        pt_lo = [sb(f"pt_lo{i}", [P, QT, S], F32R) for i in range(2)]
        o_low = sb("o_low", [P, S], F32)
        o_sum = [sb(f"o_sum{i}", [P, S], F32) for i in range(NBLK)]
        mask = sb("mask", [P, S], F32)
        ident = sb("ident", [P, P], F32)
        row_min = sb("row_min", [P, 4], F32)
        row_sum = sb("row_sum", [P, 4], F32)
        row_inv = sb("row_inv", [P, 4], F32)
        cond_bc = sb("cond_bc", [P, B], F32)
        q_scale = sb("q_scale", [P, 1], F32)

        proj_ps = [ctx.enter_context(nc.psum_tensor(f"proj_ps{i}", [P, S], F32)) for i in range(2)]
        s_ps = [ctx.enter_context(nc.psum_tensor(f"s_ps{i}", [P, S], F32)) for i in range(2)]
        t_ps = [ctx.enter_context(nc.psum_tensor(f"t_ps{i}", [P, S], F32)) for i in range(2)]
        o_ps = [ctx.enter_context(nc.psum_tensor(f"o_ps{i}", [P, S], F32)) for i in range(2)]

        const_ready = sem("const_ready")
        cond_in = sem("cond_in")
        scale_ready = sem("scale_ready")
        w_in = [sem(f"w{n}_in") for n in "qkv"]
        wqk_hi_done = sem("wqk_hi_done")
        wqk_lo_done = sem("wqk_lo_done")
        wv_hi_done = sem("wv_hi_done")
        wv_lo_done = sem("wv_lo_done")
        x_in = [sem(f"x_in{i}") for i in range(4)]
        x_hi_done = sem("x_hi_done")
        x_lo_done = [sem(f"x_lo_done{i}") for i in range(2)]
        x_free = sem("x_free")
        proj_done = sem("proj_done")
        proj_hi_done = sem("proj_hi_done")
        proj_lo_done = sem("proj_lo_done")
        k_swapped = [sem(f"k_swapped{i}") for i in range(NBLK)]
        s_done = sem("s_done")
        max_may_start = sem("max_may_start")
        max_done = sem("max_done")
        exp_done = sem("exp_done")
        inv_done = sem("inv_done")
        norm_done = sem("norm_done")
        t_done = sem("t_done")
        pt_hi_done = sem("pt_hi_done")
        pt_lo_done = sem("pt_lo_done")
        pv_done = sem("pv_done")
        o_low_done = sem("o_low_done")
        o_sum_done = [sem(f"o_sum_done{i}") for i in range(2)]
        o_out = [sem(f"o_out{i}") for i in range(NBLK)]

        groups = [("q", 0), ("k", 0), ("q", 1), ("k", 1)] + [("v", t) for t in range(QT)]
        NPROJ = len(groups)
        start = [16 * 2 * i / 12 for i in range(4)] + [16 * (8 + i) / 12 for i in range(QT)]
        length = [16 * 2 / 12] * 4 + [16 / 12] * QT
        EVAC = [2, 4, 6, 8, 9, 10, 11, 12]
        NEV = EVAC[-1]

        S_AT = 8.7
        T_AT = S_AT + 2.1
        PV_AT = [17.4, 20.0, 22.8, 26.8]

        def project(pe, it, g, gi, k):
            kind, n = groups[gi]
            bank = proj_ps[gi % 2]
            w = "qkv".index(kind)
            if k == 0:
                wait(pe, proj_lo_done, it * NEV + (EVAC[gi - 2] if gi >= 2 else EVAC[gi + NPROJ - 2] - NEV))
                if kind == "v":
                    wait(pe, wv_lo_done, g + 1)
                else:
                    wait(pe, wqk_lo_done, g * 4 + gi + 1)
            if gi == 0:
                wait(pe, x_lo_done[k % 2], it * (KT // 2) + k // 2 + 1)
            if kind == "v":
                tok = slice(n * P, (n + 1) * P)
                out = bank[:, 0:EG]
                passes = [(x_lo[:, k, tok], w_hi[w][:, k, :]), (x_hi[:, k, tok], w_lo[w][:, k, :]),
                          (x_hi[:, k, tok], w_hi[w][:, k, :])]
            else:
                col = slice(n * P, (n + 1) * P)
                out = bank[:, :]
                passes = [(w_lo[w][:, k, col], x_hi[:, k, :]), (w_hi[w][:, k, col], x_lo[:, k, :]),
                          (w_hi[w][:, k, col], x_hi[:, k, :])]
            for i, (l, r) in enumerate(passes):
                mm = pe.matmul(out, l, r, start=(k == 0 and i == 0), stop=(k == KT - 1 and i == 2))
            if gi == NPROJ - 1:
                mm.then_inc(x_free, 1)
            elif k == KT - 1:
                mm.then_inc(proj_done, 1)

        def proj_ready(eng, it, gi):
            if gi == NPROJ - 1:
                wait(eng, x_free, it * KT + KT)
            else:
                wait(eng, proj_done, it * (NPROJ - 1) + gi + 1)

        def halves(gi):
            _, blk = groups[gi]
            return [(2 * blk, slice(0, DH), slice(DH, P)), (2 * blk + 1, slice(DH, P), slice(0, DH))]

        def v_view(t, part):
            return v_st[:, t, :, part, :]

        def evac_hi(act, it, gi):
            kind, n = groups[gi]
            bank = proj_ps[gi % 2]
            proj_ready(act, it, gi)
            if kind == "v":
                if n == 0:
                    wait(act, pv_done, it * HG)
                act.activation(v_view(n, 0), bank[:, 0:EG].rearrange("p (h d) -> p h d", d=DH),
                               ACT.Copy).then_inc(proj_hi_done, 1)
                return
            wait(act, s_done, (it - 1) * UNITS + (n + 1) * 2 * QT)
            if kind == "q":
                wait(act, scale_ready, it + 1)
            for head, src, _ in halves(gi):
                if kind == "q":
                    act.activation(q_st[src, head, :], bank[src, :], ACT.Copy,
                                   scale=q_scale[src, 0:1]).then_inc(proj_hi_done, 1)
                else:
                    if head % 2 == 0:
                        wait(act, k_swapped[n], it * 32)
                    act.activation(k_st[src, head, :], bank[src, :], ACT.Copy).then_inc(proj_hi_done, 1)

        def evac_lo(dve, it, gi):
            kind, n = groups[gi]
            bank = proj_ps[gi % 2]
            if kind == "v":
                wait(dve, proj_hi_done, it * NEV + EVAC[gi])
                dve.tensor_tensor(v_view(n, 1), bank[:, 0:EG].rearrange("p (h d) -> p h d", d=DH),
                                  v_view(n, 0).bitcast(F32), ALU.subtract).then_inc(proj_lo_done, 1)
                return
            for i, (head, src, dst) in enumerate(halves(gi)):
                wait(dve, proj_hi_done, it * NEV + EVAC[gi] - 1 + i)
                if kind == "q":
                    dve.scalar_tensor_tensor(out=q_st[dst, head, :], in0=bank[src, :], scalar=q_scale[src, 0:1],
                                             in1=q_st[src, head, :].bitcast(F32), op0=ALU.mult,
                                             op1=ALU.subtract).then_inc(proj_lo_done, 1)
                else:
                    dve.tensor_tensor(k_st[dst, head, :], bank[src, :], k_st[src, head, :].bitcast(F32),
                                      ALU.subtract).then_inc(proj_lo_done, 1)

        def swap_k(sp, it, blk):
            wait(sp, proj_lo_done, it * NEV + EVAC[2 * blk + 1])
            heads = slice(2 * blk, 2 * blk + 2)
            sp.dma_start(k_sw[0:DH, heads, :].bitcast(F32), k_st[DH:P, heads, :].bitcast(F32)).then_inc(k_swapped[blk], 16)
            sp.dma_start(k_sw[DH:P, heads, :].bitcast(F32), k_st[0:DH, heads, :].bitcast(F32)).then_inc(k_swapped[blk], 16)

        def scores(pe, it, u):
            h, qt = divmod(u, QT)
            n = it * UNITS + u
            if u % (2 * QT) == 0:
                wait(pe, k_swapped[h // 2], (it + 1) * 32)
            wait(pe, max_done, n - 1)
            w = max(2 * P, (qt + 1) * P)
            q = q_st[:, h, qt * P:(qt + 1) * P]
            pe.matmul(s_ps[u % 2][:, 0:w], q, k_sw[:, h, 0:w], start=True, stop=False)
            pe.matmul(s_ps[u % 2][:, 0:w], q, k_st[:, h, 0:w], start=False, stop=True).then_inc(s_done, 1)

        def mask_max(dve, it, u):
            qt = u % QT
            n = it * UNITS + u
            w = (qt + 1) * P
            wait(dve, s_done, n + 1)
            wait(dve, t_done, n - 3)
            apart(dve, max_may_start)
            dve.tensor_tensor_reduce(prob[:, u % 4, 0:w], s_ps[u % 2][:, 0:w], mask[:, S - w:S], 1.0,
                                     -MASKED, ALU.add, ALU.min, row_min[:, u % 4:u % 4 + 1]).then_inc(max_done, 1)

        def exponent(act, it, u):
            w = (u % QT + 1) * P
            n = it * UNITS + u
            wait(act, max_done, n + 1)
            act.activation(prob[:, u % 4, 0:w], prob[:, u % 4, 0:w], ACT.Exp, bias=row_min[:, u % 4:u % 4 + 1],
                           scale=-1.0, accum_out=row_sum[:, u % 4:u % 4 + 1]).then_inc(exp_done, 1)

        def invert(dve, it, u):
            n = it * UNITS + u
            wait(dve, exp_done, n + 1)
            dve.reciprocal(row_inv[:, u % 4:u % 4 + 1], row_sum[:, u % 4:u % 4 + 1]).then_inc(inv_done, 1)

        def normalise(pool, it, u):
            w = (u % QT + 1) * P
            n = it * UNITS + u
            wait(pool, inv_done, n + 1)
            pool.tensor_tensor(prob[:, u % 4, 0:w], prob[:, u % 4, 0:w],
                               row_inv[:, u % 4:u % 4 + 1].broadcast_to([P, w]), ALU.mult).then_inc(norm_done, 1)

        def transpose(pe, it, u):
            qt = u % QT
            n = it * UNITS + u
            wait(pe, norm_done, n + 1)
            wait(pe, pt_lo_done, n - 1)
            for kb in range(qt + 1):
                mm = pe.transpose(t_ps[u % 2][:, kb * P:(kb + 1) * P], prob[:, u % 4, kb * P:(kb + 1) * P],
                                  ident[:, :])
            mm.then_inc(t_done, 1)

        def pt_view(buf, qt):
            return buf[:, 0:qt + 1, qt * P:(qt + 1) * P]

        def pt_high(act, it, u):
            h, qt = divmod(u, QT)
            n = it * UNITS + u
            wait(act, t_done, n + 1)
            if qt == 0:
                wait(act, pv_done, it * HG + h - 1)
            act.activation(pt_view(pt_hi[h % 2], qt), t_ps[u % 2][:, 0:(qt + 1) * P]
                           .rearrange("p (k q) -> p k q", q=P), ACT.Copy).then_inc(pt_hi_done, 1)

        def pt_low(dve, it, u):
            h, qt = divmod(u, QT)
            n = it * UNITS + u
            wait(dve, pt_hi_done, n + 1)
            dve.tensor_tensor(pt_view(pt_lo[h % 2], qt), t_ps[u % 2][:, 0:(qt + 1) * P]
                              .rearrange("p (k q) -> p k q", q=P), pt_view(pt_hi[h % 2], qt).bitcast(F32),
                              ALU.subtract).then_inc(pt_lo_done, 1)

        def times_v(pe, it, h):
            wait(pe, pt_lo_done, it * UNITS + (h + 1) * QT)
            if h == 0:
                wait(pe, const_ready, 4)
                wait(pe, proj_lo_done, (it + 1) * NEV)
            wait(pe, o_sum_done[h % 2], it * NBLK + h // 2 + 1)
            for kb in range(QT):
                q0 = min(kb * P, S - 2 * P)
                v = v_st[:, kb, h, :, :].rearrange("p a d -> p (a d)")
                for part in (pt_lo, pt_hi):
                    mm = pe.matmul(o_ps[h % 2][:, q0:S], v, part[h % 2][:, kb, q0:S],
                                   start=(kb == 0 and part is pt_lo), stop=(kb == QT - 1 and part is pt_hi))
            mm.then_inc(pv_done, 1)

        def o_lower(act, it, h):
            n = it * HG + h
            dst = slice(0, DH) if h % 2 == 0 else slice(DH, P)
            wait(act, pv_done, n + 1)
            wait(act, o_sum_done[h % 2], it * NBLK + h // 2 + 1)
            act.activation(o_low[dst, :], o_ps[h % 2][DH:P, :], ACT.Copy).then_inc(o_low_done, 1)

        def o_add(dve, it, h):
            n = it * HG + h
            dst = slice(0, DH) if h % 2 == 0 else slice(DH, P)
            wait(dve, o_low_done, n + 1)
            if h % 2 == 0:
                wait(dve, o_out[h // 2], it * 16 + 1)
            dve.tensor_tensor(o_sum[h // 2][dst, :], o_ps[h % 2][0:DH, :], o_low[dst, :],
                              ALU.add).then_inc(o_sum_done[h % 2], 1)

        def store_o(sp, it, g, b, blk):
            for parity in range(2):
                wait(sp, o_sum_done[parity], it * NBLK + blk + 2)
            row = g * NBLK + blk
            sp.dma_start(oT[bass.ds(row, 1), :, bass.ds(b, 1), :].rearrange("a p b s -> p (a b s)"), o_sum[blk][:, :]).then_inc(o_out[blk], 16)

        def load_x(sp, it, b):
            for half in x_lo_done:
                wait(sp, half, it * (KT // 2))
            for n, arrived in enumerate(x_in):
                ks = slice(n * KT // 4, (n + 1) * KT // 4)
                sp.dma_start(x_raw[:, ks, :], xT[bass.ds(b, 1), :, ks, :].rearrange("a p k s -> p (a k) s"))\
                  .then_inc(arrived, 16)

        def x_high(act, it, k):
            if k % 2 == 0:
                wait(act, x_in[k // 2], (it + 1) * 16)
            wait(act, x_free, (it - 1) * KT + k + 1)
            act.activation(x_hi[:, k, :], x_raw[:, k, :], ACT.Copy).then_inc(x_hi_done, 1)

        def x_low(eng, it, k):
            wait(eng, x_hi_done, it * KT + k + 1)
            eng.tensor_tensor(x_lo[:, k, :], x_raw[:, k, :], x_hi[:, k, :].bitcast(F32),
                              ALU.subtract).then_inc(x_lo_done[k % 2], 1)

        def batch_scale(dve, it, b):
            if isinstance(it, int) and it == 0:
                wait(dve, cond_in, 16)
            else:
                wait(dve, proj_lo_done, (it - 1) * NEV + EVAC[2])
            dve.tensor_scalar(q_scale[:, 0:1], cond_bc[:, bass.ds(b, 1)], 4.0, -float(DH) ** -0.5,
                              ALU.min, ALU.mult).then_inc(scale_ready, 1)

        def load_w(sp, g, which):
            wait(sp, wv_lo_done, g)
            for n in which:
                sp.dma_start(w_raw[n][:, :, :], (wq, wk, wv)[n][bass.ds(g, 1), :, :, :]
                             .rearrange("a p k e -> p (a k) e")).then_inc(w_in[n], 16)

        def split_w_qk(eng, it, g, gi, low):
            kind, blk = groups[gi]
            w = "qkv".index(kind)
            cols = slice(blk * P, (blk + 1) * P)
            if low:
                wait(eng, wqk_hi_done, g * 4 + gi + 1)
                eng.tensor_tensor(w_lo[w][:, :, cols], w_raw[w][:, :, cols], w_hi[w][:, :, cols].bitcast(F32),
                                  ALU.subtract).then_inc(wqk_lo_done, 1)
            else:
                wait(eng, w_in[w], (g + 1) * 16)
                wait(eng, proj_done, it * (NPROJ - 1) + gi + 1)
                eng.activation(w_hi[w][:, :, cols], w_raw[w][:, :, cols], ACT.Copy).then_inc(wqk_hi_done, 1)

        def split_w_v(eng, it, g, low):
            if low:
                wait(eng, wv_hi_done, g + 1)
                eng.tensor_tensor(w_lo[2][:, :, :], w_raw[2][:, :, :], w_hi[2][:, :, :].bitcast(F32),
                                  ALU.subtract).then_inc(wv_lo_done, 1)
            else:
                wait(eng, w_in[2], (g + 1) * 16)
                wait(eng, x_free, it * KT + KT)
                eng.activation(w_hi[2][:, :, :], w_raw[2][:, :, :], ACT.Copy).then_inc(wv_hi_done, 1)

        def x_at(k):
            return start[-1] + length[-1] * (k + 1) / KT + 0.05

        def step(tables, now=None, old=None, nxt=None, qk_for=None, v_for=None, first=False):
            pe, act, dve, pool, sp = (tables[n] for n in ("pe", "act", "dve", "pool", "sp"))
            if first:
                it, g, b = now
                sp.add(-9, load_w, 0, [0])
                sp.add(-8, load_x, 0, b)
                sp.add(-7, load_w, 0, [1, 2])
                dve.add(-3, batch_scale, it, b)
                for gi, at in enumerate([-2.9, 0.1, 0.5, 0.9]):
                    act.add(at, split_w_qk, -1, 0, gi, False)
                    dve.add(at, split_w_qk, -1, 0, gi, True)
                act.add(1.2, split_w_v, -1, 0, False)
                dve.add(1.2, split_w_v, -1, 0, True)
                for k in range(KT):
                    act.add(-2.8 + 0.05 * k, x_high, it, k)
                    (dve, pool)[k % 2].add(-2.7 + 0.05 * k, x_low, it, k)
            elif now is not None:
                for k in range(KT):
                    if x_at(k) >= 16:
                        act.add(x_at(k) - 16, x_high, now[0], k)
                    if x_at(k) + 0.2 >= 16:
                        (dve, pool)[k % 2].add(x_at(k) + 0.2 - 16, x_low, now[0], k)
            for who, lo, hi, shift in ((now, 0, 16, 0), (old, 16, 32, 16)):
                if who is None:
                    continue
                it, g, b = who

                def put(table, time, *args):
                    if lo <= time < hi:
                        table.add(time - shift, *args)

                for gi in range(NPROJ):
                    for k in range(KT):
                        put(pe, start[gi] + length[gi] * k / KT, project, it, g, gi, k)
                    end = start[gi] + length[gi]
                    put(act, end + 0.05, evac_hi, it, gi)
                    put(dve, end + 0.25, evac_lo, it, gi)
                for blk in range(NBLK):
                    put(sp, start[2 * blk + 1] + length[0] + 0.8, swap_k, it, blk)
                for u in range(UNITS):
                    put(pe, S_AT + u, scores, it, u)
                    put(dve, S_AT + u + 0.2, mask_max, it, u)
                    put(act, S_AT + u + 0.42, exponent, it, u)
                    put(dve, S_AT + u + 0.7, invert, it, u)
                    put(pool, S_AT + u + 0.72, normalise, it, u)
                    put(pe, T_AT + u, transpose, it, u)
                    put(act, T_AT + u + 0.25, pt_high, it, u)
                    put(dve, T_AT + u + 0.45, pt_low, it, u)
                for h in range(HG):
                    put(pe, PV_AT[h], times_v, it, h)
                    put(act, PV_AT[h] + 0.5, o_lower, it, h)
                    put(dve, PV_AT[h] + 0.75, o_add, it, h)
                for blk in range(NBLK):
                    put(sp, PV_AT[2 * blk + 1] + 1.1, store_o, it, g, b, blk)
            if nxt is not None:
                it, b = nxt
                sp.add(0.5, load_x, it, b)
                dve.add(15.2, batch_scale, it, b)
                for k in range(KT):
                    if x_at(k) < 16:
                        act.add(x_at(k), x_high, it, k)
                    if x_at(k) + 0.2 < 16:
                        (dve, pool)[k % 2].add(x_at(k) + 0.2, x_low, it, k)
            if qk_for is not None:
                sp.add(0, load_w, qk_for, [0, 1, 2])
                for gi in range(4):
                    act.add(9.0 + 1.6 * gi, split_w_qk, now[0], qk_for, gi, False)
                    dve.add(9.4 + 1.6 * gi, split_w_qk, now[0], qk_for, gi, True)
            if v_for is not None:
                act.add(1.0, split_w_v, now[0] - 1, v_for, False)
                dve.add(1.5, split_w_v, now[0] - 1, v_for, True)

        def program(eng, name):
            def emit(**what):
                tables = {n: Timetable() for n in ("pe", "act", "dve", "pool", "sp")}
                step(tables, **what)
                tables[name].run(eng)

            def middle(g):
                with eng.Fori(1, B - 1) as b:
                    it = g * B + b
                    emit(now=(it, g, b), old=(it - 1, g, b - 1), nxt=(it + 1, b + 1))

            emit(now=(0, 0, 0), nxt=(1, 1), first=True)
            middle(0)
            with eng.Fori(1, NG) as g:
                it = g * B
                emit(now=(it - 1, g - 1, B - 1), old=(it - 2, g - 1, B - 2), nxt=(it, 0), qk_for=g)
                emit(now=(it, g, 0), old=(it - 1, g - 1, B - 1), nxt=(it + 1, 1), v_for=g)
                middle(g)
            it, g = STEPS - 1, NG - 1
            emit(now=(it, g, B - 1), old=(it - 1, g, B - 2))
            emit(old=(it, g, B - 1))

        block = ctx.enter_context(nc.Block())

        @block.sync
        def _(sp):
            sp.dma_start(cond_bc[:, :], cond.rearrange("b a -> a b").broadcast_to([P, B])).then_inc(cond_in, 16)
            for free in o_sum_done + o_out:
                sp.sem_inc(free, 1)
            program(sp, "sp")
            for blk in range(NBLK):
                sp.wait_ge(o_out[blk], STEPS * 16 + 1)

        @block.tensor
        def _(pe):
            wait(pe, const_ready, 4)
            program(pe, "pe")

        @block.scalar
        def _(act):
            program(act, "act")

        @block.vector
        def _(dve):
            for i in range(2):
                dve.memset(pt_hi[i][:, QT - 1, S - 2 * P:S - P].bitcast(F32), 0.0).then_inc(const_ready, 1)
                dve.memset(pt_lo[i][:, QT - 1, S - 2 * P:S - P].bitcast(F32), 0.0).then_inc(const_ready, 1)
            wait(dve, const_ready, 8)
            program(dve, "dve")

        @block.gpsimd
        def _(pool):
            fills = const_ready
            wait(pool, fills, 4)
            pool.memset(ident[:, :], 0.0).then_inc(fills, 1)
            pool.memset(mask[:, :], 0.0).then_inc(fills, 1)
            wait(pool, fills, 6)
            pool.affine_select(out=ident[:, :], in_=ident[:, :], compare_op=ALU.not_equal, fill=1.0, base=0,
                               pattern=[[-1, P]], channel_multiplier=1).then_inc(fills, 1)
            pool.affine_select(out=mask[:, S - P:S], in_=mask[:, S - P:S], compare_op=ALU.is_ge, fill=-MASKED,
                               base=0, pattern=[[-1, P]], channel_multiplier=1).then_inc(fills, 1)
            program(pool, "pool")


def ffn_phase(nc, x, oT, wo, wf, bias, out):
    with ExitStack() as ctx:
        def sb(name, shape, dt):
            return ctx.enter_context(nc.sbuf_tensor(name, shape, dt))

        def sem(name):
            return ctx.enter_context(nc.semaphore(name))

        HALF = D // 2
        wo_raw = sb("wo_raw", [P, KT, D], F32)
        wo_hi = sb("wo_hi", [P, KT, D], F32R)
        wo_lo = sb("wo_lo", [P, KT, D], F32R)
        wf_raw = wo_raw
        wf_q = sb("wf_q", [P, KT, D], BF16)
        o_raw = sb("o_raw", [P, 2, KT, P], F32)
        o_hi = sb("o_hi", [P, 2, KT, P], F32R)
        o_lo = sb("o_lo", [P, 2, KT, P], F32R)
        y_int = sb("y_int", [P, D], F32)
        y_q = sb("y_q", [P, 2, D], BF16)
        yt_q = sb("yt_q", [P, 2, KT, P], BF16)
        x_in_sb = sb("x_in_sb", [P, 2, D], F32)
        x_bias = sb("x_bias", [P, 2, D], F32)
        res = sb("res", [P, 2, D], F32)
        bias_bc = sb("bias_bc", [P, D], F32)
        identb = sb("identb", [P, P], BF16)
        ones = sb("ones", [P, P], F32)
        stats = sb("stats", [P, 8], F32)
        wabs = sb("wabs", [P, 1], F32)
        alpha = sb("alpha", [P, 2], F32)

        y_ps = [ctx.enter_context(nc.psum_tensor(f"y_ps{i}", [P, D], F32)) for i in range(2)]
        yt_ps = ctx.enter_context(nc.psum_tensor("yt_ps", [P, 2 * D], BF16))
        f_ps = ctx.enter_context(nc.psum_tensor("f_ps", [P, D], F32))

        consts = sem("consts")
        wo_in = sem("wo_in")
        wo_hi_done = sem("wo_hi_done")
        wo_lo_done = sem("wo_lo_done")
        wf_in = sem("wf_in")
        wf_sum = sem("wf_sum")
        wf_total = sem("wf_total")
        wf_chain = sem("wf_chain")
        bias_in = sem("bias_in")
        o_in = [sem(f"o_in{i}") for i in range(2)]
        o_hi_done = sem("o_hi_done")
        o_lo_done = sem("o_lo_done")
        x_in = [sem(f"x_in{i}") for i in range(2)]
        x_bias_done = sem("x_bias_done")
        y_done = sem("y_done")
        q_chain = sem("q_chain")
        scale_done = sem("scale_done")
        y_free = sem("y_free")
        yq_done = sem("yq_done")
        yt_done = sem("yt_done")
        ytq_done = sem("ytq_done")
        f_done = sem("f_done")
        res_done = sem("res_done")
        out_done = [sem(f"out_done{i}") for i in range(2)]

        def attention_out(pe, t, p, half):
            if half == 0:
                wait(pe, o_lo_done, t + 1)
                wait(pe, y_free, t - 1)
            for k in range(KT):
                if isinstance(t, int) and t == 0 and half == 0:
                    wait(pe, wo_lo_done, k + 1)
                w = slice(half * HALF, (half + 1) * HALF)
                for i, (o, ww) in enumerate(((o_lo, wo_hi), (o_hi, wo_lo), (o_hi, wo_hi))):
                    mm = pe.matmul(y_ps[p][:, w], o[:, p, k, :], ww[:, k, w],
                                   start=(k == 0 and i == 0), stop=(k == KT - 1 and i == 2))
            mm.then_inc(y_done, 1)

        def transpose_y(pe, t, p):
            wait(pe, yq_done, t + 1)
            wait(pe, ytq_done, t)
            for k in range(KT):
                mm = pe.transpose(yt_ps[:, k * P:(k + 1) * P], y_q[:, p, k * P:(k + 1) * P], identb[:, :])
            mm.then_inc(yt_done, 1)

        def ternary(pe, t, p):
            wait(pe, ytq_done, t + 1)
            wait(pe, res_done, t)
            if isinstance(t, int) and t == 0:
                wait(pe, wf_chain, WF_DONE)
            for half in range(2):
                w = slice(half * HALF, (half + 1) * HALF)
                for k in range(KT):
                    mm = pe.matmul(f_ps[:, w], yt_q[:, p, k, :], wf_q[:, k, w], start=(k == 0), stop=(k == KT - 1))
            mm.then_inc(f_done, 1)

        QC = 3

        def quantise(dve, t, p):
            lo, hi, sc, inv = 3 * p, 3 * p + 1, 3 * p + 2, 6 + p
            for half in range(2):
                wait(dve, y_done, 2 * t + half + 1)
                r = dve.tensor_reduce(stats[:, lo + half:lo + half + 1], y_ps[p][:, half * HALF:(half + 1) * HALF],
                                      AX.X, ALU.max, apply_absolute_value=True)
            r.then_inc(q_chain, 1)
            n = t * 6
            wait(dve, q_chain, n + 1)
            dve.tensor_tensor(stats[:, sc:sc + 1], stats[:, lo:lo + 1], stats[:, hi:hi + 1], ALU.max)\
               .then_inc(q_chain, 1)
            wait(dve, q_chain, n + 2)
            dve.tensor_scalar(stats[:, sc:sc + 1], stats[:, sc:sc + 1], EPS, 1.0 / 127.0, ALU.max, ALU.mult)\
               .then_inc(q_chain, 1)
            wait(dve, q_chain, n + 3)
            dve.reciprocal(stats[:, inv:inv + 1], stats[:, sc:sc + 1]).then_inc(q_chain, 1)
            wait(dve, q_chain, n + 4)
            dve.tensor_scalar(y_int[:, :], y_ps[p][:, :], stats[:, inv:inv + 1], MAGIC, ALU.mult, ALU.add)\
               .then_inc(y_free, 1)
            wait(dve, y_free, t + 1)
            dve.tensor_scalar(y_int[:, :], y_int[:, :], MAGIC - 128.0, MAGIC + 127.0, ALU.max, ALU.min)\
               .then_inc(q_chain, 1)
            wait(dve, q_chain, n + 5)
            wait(dve, yt_done, t - 1)
            dve.tensor_scalar(y_q[:, p, :], y_int[:, :], MAGIC, None, ALU.subtract).then_inc(yq_done, 1)
            dve.tensor_scalar(stats[:, sc:sc + 1], stats[:, sc:sc + 1], alpha[:, 0:1], None, ALU.mult)\
               .then_inc(q_chain, 1)

        def finish(dve, t, p):
            wait(dve, f_done, t + 1)
            wait(dve, q_chain, t * 6 + 6)
            wait(dve, x_bias_done, t + 1)
            wait(dve, out_done[p], PREV_OUT(t, p))
            dve.scalar_tensor_tensor(out=res[:, p, :], in0=f_ps[:, :], scalar=stats[:, 3 * p + 2:3 * p + 3],
                                     in1=x_bias[:, p, :], op0=ALU.mult, op1=ALU.add).then_inc(res_done, 1)

        def PREV_OUT(t, p):
            return (t - p) * 8

        def evac_yt(act, t, p):
            wait(act, yt_done, t + 1)
            wait(act, f_done, t - 1)
            act.activation(yt_q[:, p, :, :].rearrange("p k q -> p (k q)"), yt_ps[:, 0:D], ACT.Copy)\
               .then_inc(ytq_done, 1)

        def flat(buf, p):
            return buf[:, p, :, :].rearrange("p k q -> p (k q)")

        def split_o(pool, t, p):
            wait(pool, o_in[p], (t - p) * 8 + 16)
            wait(pool, y_done, 2 * t - 2)
            pool.tensor_tensor(flat(o_hi, p), flat(o_raw, p), ones[:, 0:1].broadcast_to([P, D]), ALU.mult).then_inc(o_hi_done, 1)
            wait(pool, o_hi_done, t + 1)
            pool.tensor_tensor(o_lo[:, p, :, :], o_raw[:, p, :, :], o_hi[:, p, :, :].bitcast(F32), ALU.subtract)\
                .then_inc(o_lo_done, 1)

        def add_bias(pool, t, p):
            if isinstance(t, int) and t == 0:
                wait(pool, bias_in, 16)
            wait(pool, x_in[p], (t - p) * 8 + 16)
            wait(pool, res_done, t - 1)
            pool.tensor_tensor(x_bias[:, p, :], x_in_sb[:, p, :], bias_bc[:, :], ALU.add).then_inc(x_bias_done, 1)

        def load_o(sp, t, p):
            wait(sp, o_lo_done, t - 1)
            sp.dma_start(o_raw[:, p, :, :], oT[:, :, :, :].rearrange("k p b s -> p k (b s)")[:, :, bass.ds(t * P, P)])\
              .then_inc(o_in[p], 16)

        def load_x(sp, t, p):
            wait(sp, x_bias_done, t - 1)
            sp.dma_start(x_in_sb[:, p, :], x[bass.ds(t * P, P), :]).then_inc(x_in[p], 16)

        def store(sp, t, p):
            wait(sp, res_done, t + 1)
            sp.dma_start(out[bass.ds(t * P, P), :], res[:, p, :]).then_inc(out_done[p], 16)

        WF_DONE = 2 + 3 * KT

        def pairs(eng, first, body, last=None):
            first()
            with eng.Fori(1, TILES // 2) as i:
                for p in range(2):
                    body(i * 2 + p, p)
            if last:
                last()

        block = ctx.enter_context(nc.Block())

        @block.sync
        def _(sp):
            for k in range(KT):
                sp.dma_start(wo_raw[:, k, :], wo[:, k, :]).then_inc(wo_in, 16)
                if k < 2:
                    load_o(sp, k, k)
            sp.dma_start(bias_bc[:, :], bias.rearrange("(a n) -> a n", a=1).broadcast_to([P, D])).then_inc(bias_in, 16)
            load_x(sp, 0, 0)
            load_x(sp, 1, 1)
            wait(sp, wo_lo_done, KT)
            sp.dma_start(wf_raw[:, :, :], wf[:, :, :]).then_inc(wf_in, 16)

            def body(t, p):
                load_o(sp, t, p)
                load_x(sp, t, p)
                store(sp, t - 2, p)
            pairs(sp, lambda: None, body)
            for p in range(2):
                store(sp, TILES - 2 + p, p)
            for p in range(2):
                sp.wait_ge(out_done[p], TILES // 2 * 16)

        @block.tensor
        def _(pe):
            wait(pe, consts, 3)

            def body(t, p):
                attention_out(pe, t, p, 0)
                transpose_y(pe, t - 1, 1 - p)
                attention_out(pe, t, p, 1)
                ternary(pe, t - 1, 1 - p)

            attention_out(pe, 0, 0, 0)
            attention_out(pe, 0, 0, 1)
            wait(pe, wf_sum, 1)
            pe.matmul(f_ps[:, 0:1], ones[:, :], wabs[:, 0:1], start=True, stop=True).then_inc(wf_total, 1)
            body(1, 1)
            pairs(pe, lambda: None, body)
            transpose_y(pe, TILES - 1, 1)
            ternary(pe, TILES - 1, 1)

        @block.scalar
        def _(act):
            for k in range(KT):
                wait(act, wo_in, KT * 16)
                act.activation(wo_hi[:, k, :], wo_raw[:, k, :], ACT.Copy).then_inc(wo_hi_done, 1)
            evac_yt(act, 0, 0)
            evac_yt(act, 1, 1)
            pairs(act, lambda: None, lambda t, p: evac_yt(act, t, p))

        @block.vector
        def _(dve):
            for k in range(KT):
                wait(dve, wo_hi_done, k + 1)
                dve.tensor_tensor(wo_lo[:, k, :], wo_raw[:, k, :], wo_hi[:, k, :].bitcast(F32), ALU.subtract)\
                   .then_inc(wo_lo_done, 1)
            wait(dve, wf_in, 16)
            dve.tensor_reduce(wabs[:, 0:1], wf_raw[:, :, :], AX.XY, ALU.add, apply_absolute_value=True)\
               .then_inc(wf_sum, 1)
            wait(dve, wf_total, 1)
            dve.tensor_scalar(alpha[:, 0:1], f_ps[:, 0:1], 1.0 / (D * D), EPS, ALU.mult, ALU.max)\
               .then_inc(wf_chain, 1)
            wait(dve, wf_chain, 1)
            dve.reciprocal(alpha[:, 1:2], alpha[:, 0:1]).then_inc(wf_chain, 1)
            wait(dve, wf_chain, 2)
            n = 2
            for k in range(KT):
                dve.tensor_scalar(wf_raw[:, k, :], wf_raw[:, k, :], alpha[:, 1:2], MAGIC, ALU.mult, ALU.add)\
                   .then_inc(wf_chain, 1)
                wait(dve, wf_chain, n + 1)
                dve.tensor_scalar(wf_raw[:, k, :], wf_raw[:, k, :], MAGIC, 1.0, ALU.subtract, ALU.min)\
                   .then_inc(wf_chain, 1)
                wait(dve, wf_chain, n + 2)
                dve.tensor_scalar(wf_q[:, k, :], wf_raw[:, k, :], -1.0, None, ALU.max).then_inc(wf_chain, 1)
                n += 3
            dve.engine_nop() if False else None
            quantise(dve, 0, 0)
            quantise(dve, 1, 1)
            finish(dve, 0, 0)

            def body(t, p):
                quantise(dve, t, p)
                finish(dve, t - 1, 1 - p)
            pairs(dve, lambda: None, body)
            finish(dve, TILES - 1, 1)

        @block.gpsimd
        def _(pool):
            pool.memset(ones[:, :], 1.0).then_inc(consts, 1)
            pool.memset(identb[:, :], 0.0).then_inc(consts, 1)
            wait(pool, consts, 2)
            pool.affine_select(out=identb[:, :], in_=identb[:, :], compare_op=ALU.not_equal, fill=1.0, base=0,
                               pattern=[[-1, P]], channel_multiplier=1).then_inc(consts, 1)

            def body(t, p):
                split_o(pool, t, p)
                add_bias(pool, t, p)

            split_o(pool, 0, 0)
            split_o(pool, 1, 1)
            add_bias(pool, 0, 0)
            add_bias(pool, 1, 1)
            pairs(pool, lambda: None, body)


def adaln_ffn_kernel(nc, x, xT, cond, wq, wk, wv, wo, wf, bias, out):
    oT = nc.dram_tensor("oT_scratch", (KT, P, B, S), F32, kind="Internal").ap()
    attention_phase(nc, xT, cond, wq, wk, wv, oT)
    ffn_phase(nc, x, oT, wo, wf, bias, out)


def kernel(x, cond_1, L0_cond_Wq, L0_cond_Wk, L0_cond_Wv, L0_cond_Wo, L0_ffn_weight, L0_ffn_bias):
    import numpy as np
    import concourse.bacc as bacc
    from concourse.bass_utils import run_bass_kernel_spmd

    def grouped(w):
        return np.ascontiguousarray(np.asarray(w).reshape(NG, EG, P, KT).transpose(0, 2, 3, 1))

    def tiled(w):
        return np.ascontiguousarray(np.asarray(w).reshape(D, KT, P).transpose(2, 1, 0))

    arrays = {
        "x": np.ascontiguousarray(x).reshape(B * S, D),
        "xT": np.ascontiguousarray(np.asarray(x).reshape(B, S, P, KT).transpose(0, 2, 3, 1)),
        "cond": np.ascontiguousarray(cond_1),
        "wq": grouped(L0_cond_Wq), "wk": grouped(L0_cond_Wk), "wv": grouped(L0_cond_Wv),
        "wo": tiled(L0_cond_Wo), "wf": tiled(L0_ffn_weight),
        "bias": np.ascontiguousarray(L0_ffn_bias),
    }
    nc = bacc.Bacc("TRN2", target_bir_lowering=False, num_devices=1)
    args = [nc.dram_tensor(n, a.shape, F32, kind="ExternalInput").ap() for n, a in arrays.items()]
    out = nc.dram_tensor("out", (B * S, D), F32, kind="ExternalOutput").ap()
    adaln_ffn_kernel(nc, *args, out)
    r = run_bass_kernel_spmd(nc, [arrays], core_ids=[0])
    return r.results[0]["out"].reshape(B, S, D)
```

```python
import concourse.bass as bass
from concourse import mybir
from contextlib import ExitStack

F32 = mybir.dt.float32
F32R = mybir.dt.float32r
BF16 = mybir.dt.bfloat16
ALU = mybir.AluOpType
ACT = mybir.ActivationFunctionType
AX = mybir.AxisListType

P = 128
B, S, D = 8, 512, 1024
DH = 64
KT = D // P
HG = 4
NG = D // DH // HG
EG = HG * DH
NBLK = HG // 2
QT = S // P
UNITS = HG * QT
STEPS = NG * B
MASKED = -3.0e38
EPS = 1e-5
MAGIC = 12582912.0
TILES = B * S // P


class Timetable:

    SLOTS = 16

    def __init__(self):
        self.entries = []

    def add(self, time, emit, *args):
        self.entries.append((time, len(self.entries), emit, args))

    def run(self, eng):
        for _, _, emit, args in sorted(self.entries, key=lambda x: x[:2]):
            emit(eng, *args)


def wait(eng, sem, value):
    if isinstance(value, int) and value <= 0:
        return
    eng.wait_ge(sem, value)


def apart(eng, passed):
    eng.sem_inc(passed, 1)


def adaln_ffn_kernel(nc, x, xT, cond, wq, wk, wv, wo, wf, bias, out):
    oT = nc.dram_tensor("oT_scratch", (KT, P, B, S), F32, kind="Internal").ap()
    with ExitStack() as ctx:
        def sb(name, shape, dt, scope=ctx):
            return scope.enter_context(nc.sbuf_tensor(name, shape, dt))

        def sem(name):
            return ctx.enter_context(nc.semaphore(name))

        WP = KT * EG
        parts = sb("parts", [P, 6 * WP + 2 * KT * S], F32R)
        w_part = [parts[:, i * WP:(i + 1) * WP].rearrange("p (k e) -> p k e", e=EG) for i in range(6)]
        w_hi, w_lo = w_part[0::2], w_part[1::2]
        x_hi = parts[:, 6 * WP:6 * WP + KT * S].rearrange("p (k s) -> p k s", s=S)
        x_lo = parts[:, 6 * WP + KT * S:].rearrange("p (k s) -> p k s", s=S)
        w_raw_all = sb("w_raw", [P, 3 * WP], F32)
        w_raw = [w_raw_all[:, i * WP:(i + 1) * WP].rearrange("p (k e) -> p k e", e=EG) for i in range(3)]
        x_raw_all = sb("x_raw", [P, KT * S], F32)
        x_raw = x_raw_all[:, :].rearrange("p (k s) -> p k s", s=S)

        assert 2 * D == WP and KT * D * 2 == 6 * WP + KT * S
        wo_hi = [parts[:, 2 * k * D:(2 * k + 1) * D] for k in range(KT)]
        wo_lo = [parts[:, (2 * k + 1) * D:(2 * k + 2) * D] for k in range(KT)]
        o_parts = parts[:, 2 * KT * D:].rearrange("p (a t n) -> p a t n", a=2, t=2)
        o_hi = [o_parts[:, 0, i, :] for i in range(2)]
        o_lo = [o_parts[:, 1, i, :] for i in range(2)]
        wf_q = w_raw_all[:, 0:2 * WP].bitcast(BF16).rearrange("p (k n) -> p k n", n=D)
        wf_raw = [w_raw_all[:, 2 * WP + i * D:2 * WP + (i + 1) * D] for i in range(2)]
        wo_raw = [x_raw_all[:, i * D:(i + 1) * D] for i in range(2)]
        o_raw = [x_raw_all[:, (2 + i) * D:(3 + i) * D] for i in range(2)]
        y_q = [x_raw_all[:, i * D // 2:(i + 1) * D // 2].bitcast(BF16) for i in range(2)]
        y_int = sb("y_int", [P, D], F32)
        identb = sb("identb", [P, P], BF16)
        one = sb("one", [P, 1], F32)
        stats = sb("stats", [P, 8], F32)
        wf_sums = sb("wf_sums", [P, KT], F32)
        wf_totals = sb("wf_totals", [P, KT], F32)
        alpha = sb("alpha", [P, 3], F32)
        ident = sb("ident", [P, P], F32)
        mask = sb("mask", [P, S], F32)

        one_ctx = ExitStack()
        pt_hi = [sb(f"pt_hi{i}", [P, QT, S], F32R, one_ctx) for i in range(2)]
        pt_lo = [sb(f"pt_lo{i}", [P, QT, S], F32R, one_ctx) for i in range(2)]
        q_st = sb("q_st", [P, HG, S], F32R, one_ctx)
        k_st = sb("k_st", [P, HG, S], F32R, one_ctx)
        k_sw = sb("k_sw", [P, HG, S], F32R, one_ctx)
        v_st = sb("v_st", [P, QT, HG, 2, DH], F32R, one_ctx)
        prob = sb("prob", [P, 4, S], F32, one_ctx)
        o_low = sb("o_low", [P, S], F32, one_ctx)
        o_sum = [sb(f"o_sum{i}", [P, S], F32, one_ctx) for i in range(NBLK)]
        row_min = sb("row_min", [P, 4], F32, one_ctx)
        row_sum = sb("row_sum", [P, 4], F32, one_ctx)
        row_inv = sb("row_inv", [P, 4], F32, one_ctx)
        cond_bc = sb("cond_bc", [P, B], F32, one_ctx)
        q_scale = sb("q_scale", [P, 1], F32, one_ctx)
        one_ctx.close()

        yt_q = sb("yt_q", [P, 2, KT, P], BF16)
        x_tile = sb("x_tile", [P, 2, D], F32)
        x_bias = sb("x_bias", [P, 2, D], F32)
        res = sb("res", [P, 2, D], F32)
        bias_bc = sb("bias_bc", [P, D], F32)

        proj_ps = [ctx.enter_context(nc.psum_tensor(f"proj_ps{i}", [P, S], F32)) for i in range(2)]
        s_ps = [ctx.enter_context(nc.psum_tensor(f"s_ps{i}", [P, S], F32)) for i in range(2)]
        t_ps = [ctx.enter_context(nc.psum_tensor(f"t_ps{i}", [P, S], F32)) for i in range(2)]
        o_ps = [ctx.enter_context(nc.psum_tensor(f"o_ps{i}", [P, S], F32)) for i in range(2)]

        const_ready = sem("const_ready")
        cond_in = sem("cond_in")
        scale_ready = sem("scale_ready")
        w_in = [sem(f"w{n}_in") for n in "qkv"]
        wqk_hi_done = sem("wqk_hi_done")
        wqk_lo_done = sem("wqk_lo_done")
        wv_hi_done = sem("wv_hi_done")
        wv_lo_done = sem("wv_lo_done")
        x_in = [sem(f"x_in{i}") for i in range(4)]
        x_hi_done = sem("x_hi_done")
        x_lo_done = [sem(f"x_lo_done{i}") for i in range(2)]
        x_free = sem("x_free")
        proj_done = sem("proj_done")
        proj_hi_done = sem("proj_hi_done")
        proj_lo_done = sem("proj_lo_done")
        k_swapped = [sem(f"k_swapped{i}") for i in range(NBLK)]
        s_done = sem("s_done")
        max_may_start = sem("max_may_start")
        max_done = sem("max_done")
        exp_done = sem("exp_done")
        inv_done = sem("inv_done")
        norm_done = sem("norm_done")
        t_done = sem("t_done")
        pt_hi_done = sem("pt_hi_done")
        pt_lo_done = sem("pt_lo_done")
        pv_done = sem("pv_done")
        o_low_done = sem("o_low_done")
        o_sum_done = [sem(f"o_sum_done{i}") for i in range(2)]
        o_out = [sem(f"o_out{i}") for i in range(NBLK)]

        groups = [("q", 0), ("k", 0), ("q", 1), ("k", 1)] + [("v", t) for t in range(QT)]
        NPROJ = len(groups)
        start = [16 * 2 * i / 12 for i in range(4)] + [16 * (8 + i) / 12 for i in range(QT)]
        length = [16 * 2 / 12] * 4 + [16 / 12] * QT
        EVAC = [2, 4, 6, 8, 9, 10, 11, 12]
        NEV = EVAC[-1]

        S_AT = 8.7
        T_AT = S_AT + 2.1
        PV_AT = [17.4, 20.0, 22.8, 26.8]

        def project(pe, it, g, gi, k):
            kind, n = groups[gi]
            bank = proj_ps[gi % 2]
            w = "qkv".index(kind)
            if k == 0:
                wait(pe, proj_lo_done, it * NEV + (EVAC[gi - 2] if gi >= 2 else EVAC[gi + NPROJ - 2] - NEV))
                if kind == "v":
                    wait(pe, wv_lo_done, g + 1)
                else:
                    wait(pe, wqk_lo_done, g * 4 + gi + 1)
            if gi == 0:
                wait(pe, x_lo_done[k % 2], it * (KT // 2) + k // 2 + 1)
            if kind == "v":
                tok = slice(n * P, (n + 1) * P)
                out = bank[:, 0:EG]
                passes = [(x_lo[:, k, tok], w_hi[w][:, k, :]), (x_hi[:, k, tok], w_lo[w][:, k, :]),
                          (x_hi[:, k, tok], w_hi[w][:, k, :])]
            else:
                col = slice(n * P, (n + 1) * P)
                out = bank[:, :]
                passes = [(w_lo[w][:, k, col], x_hi[:, k, :]), (w_hi[w][:, k, col], x_lo[:, k, :]),
                          (w_hi[w][:, k, col], x_hi[:, k, :])]
            for i, (l, r) in enumerate(passes):
                mm = pe.matmul(out, l, r, start=(k == 0 and i == 0), stop=(k == KT - 1 and i == 2))
            if gi == NPROJ - 1:
                mm.then_inc(x_free, 1)
            elif k == KT - 1:
                mm.then_inc(proj_done, 1)

        def proj_ready(eng, it, gi):
            if gi == NPROJ - 1:
                wait(eng, x_free, it * KT + KT)
            else:
                wait(eng, proj_done, it * (NPROJ - 1) + gi + 1)

        def halves(gi):
            _, blk = groups[gi]
            return [(2 * blk, slice(0, DH), slice(DH, P)), (2 * blk + 1, slice(DH, P), slice(0, DH))]

        def v_view(t, part):
            return v_st[:, t, :, part, :]

        def evac_hi(act, it, gi):
            kind, n = groups[gi]
            bank = proj_ps[gi % 2]
            proj_ready(act, it, gi)
            if kind == "v":
                if n == 0:
                    wait(act, pv_done, it * HG)
                act.activation(v_view(n, 0), bank[:, 0:EG].rearrange("p (h d) -> p h d", d=DH),
                               ACT.Copy).then_inc(proj_hi_done, 1)
                return
            wait(act, s_done, (it - 1) * UNITS + (n + 1) * 2 * QT)
            if kind == "q":
                wait(act, scale_ready, it + 1)
            for head, src, _ in halves(gi):
                if kind == "q":
                    act.activation(q_st[src, head, :], bank[src, :], ACT.Copy,
                                   scale=q_scale[src, 0:1]).then_inc(proj_hi_done, 1)
                else:
                    if head % 2 == 0:
                        wait(act, k_swapped[n], it * 32)
                    act.activation(k_st[src, head, :], bank[src, :], ACT.Copy).then_inc(proj_hi_done, 1)

        def evac_lo(dve, it, gi):
            kind, n = groups[gi]
            bank = proj_ps[gi % 2]
            if kind == "v":
                wait(dve, proj_hi_done, it * NEV + EVAC[gi])
                dve.tensor_tensor(v_view(n, 1), bank[:, 0:EG].rearrange("p (h d) -> p h d", d=DH),
                                  v_view(n, 0).bitcast(F32), ALU.subtract).then_inc(proj_lo_done, 1)
                return
            for i, (head, src, dst) in enumerate(halves(gi)):
                wait(dve, proj_hi_done, it * NEV + EVAC[gi] - 1 + i)
                if kind == "q":
                    dve.scalar_tensor_tensor(out=q_st[dst, head, :], in0=bank[src, :], scalar=q_scale[src, 0:1],
                                             in1=q_st[src, head, :].bitcast(F32), op0=ALU.mult,
                                             op1=ALU.subtract).then_inc(proj_lo_done, 1)
                else:
                    dve.tensor_tensor(k_st[dst, head, :], bank[src, :], k_st[src, head, :].bitcast(F32),
                                      ALU.subtract).then_inc(proj_lo_done, 1)

        def swap_k(sp, it, blk):
            wait(sp, proj_lo_done, it * NEV + EVAC[2 * blk + 1])
            heads = slice(2 * blk, 2 * blk + 2)
            sp.dma_start(k_sw[0:DH, heads, :].bitcast(F32), k_st[DH:P, heads, :].bitcast(F32)).then_inc(k_swapped[blk], 16)
            sp.dma_start(k_sw[DH:P, heads, :].bitcast(F32), k_st[0:DH, heads, :].bitcast(F32)).then_inc(k_swapped[blk], 16)

        def scores(pe, it, u):
            h, qt = divmod(u, QT)
            n = it * UNITS + u
            if u % (2 * QT) == 0:
                wait(pe, k_swapped[h // 2], (it + 1) * 32)
            wait(pe, max_done, n - 1)
            w = max(2 * P, (qt + 1) * P)
            q = q_st[:, h, qt * P:(qt + 1) * P]
            pe.matmul(s_ps[u % 2][:, 0:w], q, k_sw[:, h, 0:w], start=True, stop=False)
            pe.matmul(s_ps[u % 2][:, 0:w], q, k_st[:, h, 0:w], start=False, stop=True).then_inc(s_done, 1)

        def mask_max(dve, it, u):
            qt = u % QT
            n = it * UNITS + u
            w = (qt + 1) * P
            wait(dve, s_done, n + 1)
            wait(dve, t_done, n - 3)
            apart(dve, max_may_start)
            dve.tensor_tensor_reduce(prob[:, u % 4, 0:w], s_ps[u % 2][:, 0:w], mask[:, S - w:S], 1.0,
                                     -MASKED, ALU.add, ALU.min, row_min[:, u % 4:u % 4 + 1]).then_inc(max_done, 1)

        def exponent(act, it, u):
            w = (u % QT + 1) * P
            n = it * UNITS + u
            wait(act, max_done, n + 1)
            act.activation(prob[:, u % 4, 0:w], prob[:, u % 4, 0:w], ACT.Exp, bias=row_min[:, u % 4:u % 4 + 1],
                           scale=-1.0, accum_out=row_sum[:, u % 4:u % 4 + 1]).then_inc(exp_done, 1)

        def invert(dve, it, u):
            n = it * UNITS + u
            wait(dve, exp_done, n + 1)
            dve.reciprocal(row_inv[:, u % 4:u % 4 + 1], row_sum[:, u % 4:u % 4 + 1]).then_inc(inv_done, 1)

        def normalise(pool, it, u):
            w = (u % QT + 1) * P
            n = it * UNITS + u
            wait(pool, inv_done, n + 1)
            pool.tensor_tensor(prob[:, u % 4, 0:w], prob[:, u % 4, 0:w],
                               row_inv[:, u % 4:u % 4 + 1].broadcast_to([P, w]), ALU.mult).then_inc(norm_done, 1)

        def transpose(pe, it, u):
            qt = u % QT
            n = it * UNITS + u
            wait(pe, norm_done, n + 1)
            wait(pe, pt_lo_done, n - 1)
            for kb in range(qt + 1):
                mm = pe.transpose(t_ps[u % 2][:, kb * P:(kb + 1) * P], prob[:, u % 4, kb * P:(kb + 1) * P],
                                  ident[:, :])
            mm.then_inc(t_done, 1)

        def pt_view(buf, qt):
            return buf[:, 0:qt + 1, qt * P:(qt + 1) * P]

        def pt_high(act, it, u):
            h, qt = divmod(u, QT)
            n = it * UNITS + u
            wait(act, t_done, n + 1)
            if qt == 0:
                wait(act, pv_done, it * HG + h - 1)
            act.activation(pt_view(pt_hi[h % 2], qt), t_ps[u % 2][:, 0:(qt + 1) * P]
                           .rearrange("p (k q) -> p k q", q=P), ACT.Copy).then_inc(pt_hi_done, 1)

        def pt_low(dve, it, u):
            h, qt = divmod(u, QT)
            n = it * UNITS + u
            wait(dve, pt_hi_done, n + 1)
            dve.tensor_tensor(pt_view(pt_lo[h % 2], qt), t_ps[u % 2][:, 0:(qt + 1) * P]
                              .rearrange("p (k q) -> p k q", q=P), pt_view(pt_hi[h % 2], qt).bitcast(F32),
                              ALU.subtract).then_inc(pt_lo_done, 1)

        def times_v(pe, it, h):
            wait(pe, pt_lo_done, it * UNITS + (h + 1) * QT)
            if h == 0:
                wait(pe, const_ready, 4)
                wait(pe, proj_lo_done, (it + 1) * NEV)
            wait(pe, o_sum_done[h % 2], it * NBLK + h // 2 + 1)
            for kb in range(QT):
                q0 = min(kb * P, S - 2 * P)
                v = v_st[:, kb, h, :, :].rearrange("p a d -> p (a d)")
                for part in (pt_lo, pt_hi):
                    mm = pe.matmul(o_ps[h % 2][:, q0:S], v, part[h % 2][:, kb, q0:S],
                                   start=(kb == 0 and part is pt_lo), stop=(kb == QT - 1 and part is pt_hi))
            mm.then_inc(pv_done, 1)

        def o_lower(act, it, h):
            n = it * HG + h
            dst = slice(0, DH) if h % 2 == 0 else slice(DH, P)
            wait(act, pv_done, n + 1)
            wait(act, o_sum_done[h % 2], it * NBLK + h // 2 + 1)
            act.activation(o_low[dst, :], o_ps[h % 2][DH:P, :], ACT.Copy).then_inc(o_low_done, 1)

        def o_add(dve, it, h):
            n = it * HG + h
            dst = slice(0, DH) if h % 2 == 0 else slice(DH, P)
            wait(dve, o_low_done, n + 1)
            if h % 2 == 0:
                wait(dve, o_out[h // 2], it * 16 + 1)
            dve.tensor_tensor(o_sum[h // 2][dst, :], o_ps[h % 2][0:DH, :], o_low[dst, :],
                              ALU.add).then_inc(o_sum_done[h % 2], 1)

        def store_o(sp, it, g, b, blk):
            for parity in range(2):
                wait(sp, o_sum_done[parity], it * NBLK + blk + 2)
            row = g * NBLK + blk
            sp.dma_start(oT[bass.ds(row, 1), :, bass.ds(b, 1), :].rearrange("a p b s -> p (a b s)"), o_sum[blk][:, :]).then_inc(o_out[blk], 16)

        def load_x(sp, it, b):
            for half in x_lo_done:
                wait(sp, half, it * (KT // 2))
            for n, arrived in enumerate(x_in):
                ks = slice(n * KT // 4, (n + 1) * KT // 4)
                sp.dma_start(x_raw[:, ks, :], xT[bass.ds(b, 1), :, ks, :].rearrange("a p k s -> p (a k) s"))\
                  .then_inc(arrived, 16)

        def x_high(act, it, k):
            if k % 2 == 0:
                wait(act, x_in[k // 2], (it + 1) * 16)
            wait(act, x_free, (it - 1) * KT + k + 1)
            act.activation(x_hi[:, k, :], x_raw[:, k, :], ACT.Copy).then_inc(x_hi_done, 1)

        def x_low(eng, it, k):
            wait(eng, x_hi_done, it * KT + k + 1)
            eng.tensor_tensor(x_lo[:, k, :], x_raw[:, k, :], x_hi[:, k, :].bitcast(F32),
                              ALU.subtract).then_inc(x_lo_done[k % 2], 1)

        def batch_scale(dve, it, b):
            if isinstance(it, int) and it == 0:
                wait(dve, cond_in, 16)
            else:
                wait(dve, proj_lo_done, (it - 1) * NEV + EVAC[2])
            dve.tensor_scalar(q_scale[:, 0:1], cond_bc[:, bass.ds(b, 1)], 4.0, -float(DH) ** -0.5,
                              ALU.min, ALU.mult).then_inc(scale_ready, 1)

        def load_w(sp, g, which):
            wait(sp, wv_lo_done, g)
            for n in which:
                sp.dma_start(w_raw[n][:, :, :], (wq, wk, wv)[n][bass.ds(g, 1), :, :, :]
                             .rearrange("a p k e -> p (a k) e")).then_inc(w_in[n], 16)

        def split_w_qk(eng, it, g, gi, low):
            kind, blk = groups[gi]
            w = "qkv".index(kind)
            cols = slice(blk * P, (blk + 1) * P)
            if low:
                wait(eng, wqk_hi_done, g * 4 + gi + 1)
                eng.tensor_tensor(w_lo[w][:, :, cols], w_raw[w][:, :, cols], w_hi[w][:, :, cols].bitcast(F32),
                                  ALU.subtract).then_inc(wqk_lo_done, 1)
            else:
                wait(eng, w_in[w], (g + 1) * 16)
                wait(eng, proj_done, it * (NPROJ - 1) + gi + 1)
                eng.activation(w_hi[w][:, :, cols], w_raw[w][:, :, cols], ACT.Copy).then_inc(wqk_hi_done, 1)

        def split_w_v(eng, it, g, low):
            if low:
                wait(eng, wv_hi_done, g + 1)
                eng.tensor_tensor(w_lo[2][:, :, :], w_raw[2][:, :, :], w_hi[2][:, :, :].bitcast(F32),
                                  ALU.subtract).then_inc(wv_lo_done, 1)
            else:
                wait(eng, w_in[2], (g + 1) * 16)
                wait(eng, x_free, it * KT + KT)
                eng.activation(w_hi[2][:, :, :], w_raw[2][:, :, :], ACT.Copy).then_inc(wv_hi_done, 1)

        def x_at(k):
            return start[-1] + length[-1] * (k + 1) / KT + 0.05

        def step(tables, now=None, old=None, nxt=None, qk_for=None, v_for=None, first=False, more=None):
            pe, act, dve, pool, sp = (tables[n] for n in ("pe", "act", "dve", "pool", "sp"))
            if first:
                it, g, b = now
                sp.add(-9, load_w, 0, [0])
                sp.add(-8, load_x, 0, b)
                sp.add(-7, load_w, 0, [1, 2])
                dve.add(-3, batch_scale, it, b)
                for gi, at in enumerate([-2.9, 0.1, 0.5, 0.9]):
                    act.add(at, split_w_qk, -1, 0, gi, False)
                    dve.add(at, split_w_qk, -1, 0, gi, True)
                act.add(1.2, split_w_v, -1, 0, False)
                dve.add(1.2, split_w_v, -1, 0, True)
                for k in range(KT):
                    act.add(-2.8 + 0.05 * k, x_high, it, k)
                    (dve, pool)[k % 2].add(-2.7 + 0.05 * k, x_low, it, k)
            elif now is not None:
                for k in range(KT):
                    if x_at(k) >= 16:
                        act.add(x_at(k) - 16, x_high, now[0], k)
                    if x_at(k) + 0.2 >= 16:
                        (dve, pool)[k % 2].add(x_at(k) + 0.2 - 16, x_low, now[0], k)
            for who, lo, hi, shift in ((now, 0, 16, 0), (old, 16, 32, 16)):
                if who is None:
                    continue
                it, g, b = who

                def put(table, time, *args):
                    if lo <= time < hi:
                        table.add(time - shift, *args)

                for gi in range(NPROJ):
                    for k in range(KT):
                        put(pe, start[gi] + length[gi] * k / KT, project, it, g, gi, k)
                    end = start[gi] + length[gi]
                    put(act, end + 0.05, evac_hi, it, gi)
                    put(dve, end + 0.25, evac_lo, it, gi)
                for blk in range(NBLK):
                    put(sp, start[2 * blk + 1] + length[0] + 0.8, swap_k, it, blk)
                for u in range(UNITS):
                    put(pe, S_AT + u, scores, it, u)
                    put(dve, S_AT + u + 0.2, mask_max, it, u)
                    put(act, S_AT + u + 0.42, exponent, it, u)
                    put(dve, S_AT + u + 0.7, invert, it, u)
                    put(pool, S_AT + u + 0.72, normalise, it, u)
                    put(pe, T_AT + u, transpose, it, u)
                    put(act, T_AT + u + 0.25, pt_high, it, u)
                    put(dve, T_AT + u + 0.45, pt_low, it, u)
                for h in range(HG):
                    put(pe, PV_AT[h], times_v, it, h)
                    put(act, PV_AT[h] + 0.5, o_lower, it, h)
                    put(dve, PV_AT[h] + 0.75, o_add, it, h)
                for blk in range(NBLK):
                    put(sp, PV_AT[2 * blk + 1] + 1.1, store_o, it, g, b, blk)
            if nxt is not None:
                it, b = nxt
                sp.add(0.5, load_x, it, b)
                dve.add(15.2, batch_scale, it, b)
                for k in range(KT):
                    if x_at(k) < 16:
                        act.add(x_at(k), x_high, it, k)
                    if x_at(k) + 0.2 < 16:
                        (dve, pool)[k % 2].add(x_at(k) + 0.2, x_low, it, k)
            if qk_for is not None:
                sp.add(0, load_w, qk_for, [0, 1, 2])
                for gi in range(4):
                    act.add(9.0 + 1.6 * gi, split_w_qk, now[0], qk_for, gi, False)
                    dve.add(9.4 + 1.6 * gi, split_w_qk, now[0], qk_for, gi, True)
            if v_for is not None:
                act.add(1.0, split_w_v, now[0] - 1, v_for, False)
                dve.add(1.5, split_w_v, now[0] - 1, v_for, True)
            if more is not None:
                more(**tables)

        HALF = D // 2
        y_ps = [proj_ps, s_ps]
        yt_ps = t_ps[0][:, :].bitcast(BF16)
        f_ps = o_ps

        wo_in = [sem(f"wo_in{i}") for i in range(2)]
        wo_hi_done = sem("wo_hi_done")
        wo_lo_done = sem("wo_lo_done")
        wf_in = [sem(f"wf_in{i}") for i in range(2)]
        wf_abs_done = sem("wf_abs_done")
        wf_q_done = sem("wf_q_done")
        wf_total = sem("wf_total")
        wf_chain = sem("wf_chain")
        bias_in = sem("bias_in")
        o_in = [sem(f"o_in{i}") for i in range(2)]
        o_hi_done = sem("o_hi_done")
        o_lo_done = sem("o_lo_done")
        x_tile_in = [sem(f"x_tile_in{i}") for i in range(2)]
        x_bias_done = sem("x_bias_done")
        y_done = sem("y_done")
        q_chain = sem("q_chain")
        y_free = sem("y_free")
        yq_done = sem("yq_done")
        yt_done = sem("yt_done")
        ytq_done = sem("ytq_done")
        f_done = sem("f_done")
        res_done = sem("res_done")
        out_done = [sem(f"out_done{i}") for i in range(2)]


        def load_wf(sp, n):
            if n < 2:
                wait(sp, wv_lo_done, NG)
            elif n < KT + 2:
                wait(sp, wf_abs_done, n - 1)
            else:
                wait(sp, wf_q_done, n - 1 - KT)
            sp.dma_start(wf_raw[n % 2], wf[:, n % KT, :]).then_inc(wf_in[n % 2], 16)

        def wf_abs(act, k):
            wait(act, wf_in[k % 2], (k // 2 + 1) * 16)
            act.activation(wf_raw[k % 2], wf_raw[k % 2], ACT.Abs, accum_out=wf_sums[:, k:k + 1])\
               .then_inc(wf_abs_done, 1)

        def wf_add_partitions(pool):
            wait(pool, wf_abs_done, KT)
            nc.gpsimd.partition_all_reduce(wf_totals[:, :], wf_sums[:, :], P, bass.bass_isa.ReduceOp.add)\
              .then_inc(wf_total, 1)

        def wf_scale(dve):
            wait(dve, wf_total, 1)
            dve.tensor_reduce(alpha[:, 2:3], wf_totals[:, :], AX.X, ALU.add).then_inc(wf_chain, 1)
            wait(dve, wf_chain, 1)
            dve.tensor_scalar(alpha[:, 0:1], alpha[:, 2:3], 1.0 / (D * D), EPS, ALU.mult, ALU.max)\
               .then_inc(wf_chain, 1)
            wait(dve, wf_chain, 2)
            dve.reciprocal(alpha[:, 1:2], alpha[:, 0:1]).then_inc(wf_chain, 1)
            wait(dve, wf_chain, 3)

        def wf_ternary(dve, k):
            raw = wf_raw[k % 2]
            wait(dve, wf_in[k % 2], ((KT + k) // 2 + 1) * 16)
            dve.tensor_scalar(raw, raw, alpha[:, 1:2], MAGIC, ALU.mult, ALU.add).then_inc(wf_chain, 1)
            wait(dve, wf_chain, 4 + 2 * k)
            dve.tensor_scalar(raw, raw, MAGIC, 1.0, ALU.subtract, ALU.min).then_inc(wf_chain, 1)
            wait(dve, wf_chain, 5 + 2 * k)
            dve.tensor_scalar(wf_q[:, k, :], raw, -1.0, None, ALU.max).then_inc(wf_q_done, 1)

        def load_wo(sp, k):
            if k < 2:
                for half in x_lo_done:
                    wait(sp, half, STEPS * KT // 2)
            else:
                wait(sp, wo_lo_done, k - 1)
            sp.dma_start(wo_raw[k % 2], wo[:, k, :]).then_inc(wo_in[k % 2], 16)

        def wo_high(act, k):
            if k < 4:
                wait(act, proj_done, (STEPS - 1) * (NPROJ - 1) + (3 if k < 2 else 4))
            else:
                wait(act, x_free, STEPS * KT)
            wait(act, wo_in[k % 2], (k // 2 + 1) * 16)
            act.activation(wo_hi[k], wo_raw[k % 2], ACT.Copy).then_inc(wo_hi_done, 1)

        def wo_low(dve, k):
            wait(dve, wo_hi_done, k + 1)
            dve.tensor_tensor(wo_lo[k], wo_raw[k % 2], wo_hi[k].bitcast(F32), ALU.subtract)\
               .then_inc(wo_lo_done, 1)

        def load_o(sp, t, p):
            if isinstance(t, int) and t < 2:
                for half in x_lo_done:
                    wait(sp, half, STEPS * KT // 2)
            else:
                wait(sp, o_lo_done, t - 1)
            sp.dma_start(o_raw[p].rearrange("p (k s) -> p k s", s=P),
                         oT.rearrange("k p b s -> p k (b s)")[:, :, bass.ds(t * P, P)]).then_inc(o_in[p], 16)

        def split_o(pool, t, p):
            wait(pool, o_in[p], (t - p) * 8 + 16)
            if isinstance(t, int) and t < 2:
                wait(pool, x_free, STEPS * KT)
            else:
                wait(pool, y_done, 2 * t - 2)
            pool.tensor_tensor(o_hi[p], o_raw[p], one[:, 0:1].broadcast_to([P, D]), ALU.mult).then_inc(o_hi_done, 1)
            wait(pool, o_hi_done, t + 1)
            pool.tensor_tensor(o_lo[p], o_raw[p], o_hi[p].bitcast(F32), ALU.subtract).then_inc(o_lo_done, 1)

        def attention_out(pe, t, p, half, k):
            first = isinstance(t, int) and t < 2
            if half == 0 and k == 0:
                wait(pe, o_lo_done, t + 1)
                if not first:
                    wait(pe, y_free, t - 1)
                elif t == 0:
                    wait(pe, proj_lo_done, STEPS * NEV)
                else:
                    wait(pe, max_done, STEPS * UNITS)
            if first and t == 0 and half == 0:
                wait(pe, wo_lo_done, k + 1)
            w = slice(half * HALF, (half + 1) * HALF)
            o = slice(k * P, (k + 1) * P)
            for i, (a, b) in enumerate(((o_lo, wo_hi), (o_hi, wo_lo), (o_hi, wo_hi))):
                mm = pe.matmul(y_ps[p][half][:, :], a[p][:, o], b[k][:, w],
                               start=(k == 0 and i == 0), stop=(k == KT - 1 and i == 2))
            if k == KT - 1:
                mm.then_inc(y_done, 1)

        def attention_out_half(pe, t, p, half):
            for k in range(KT):
                attention_out(pe, t, p, half, k)

        def quantise(dve, t, p):
            lo, sc, inv = 3 * p, 3 * p + 2, 6 + p
            for half in range(2):
                wait(dve, y_done, 2 * t + half + 1)
                r = dve.tensor_reduce(stats[:, lo + half:lo + half + 1], y_ps[p][half][:, :],
                                      AX.X, ALU.max, apply_absolute_value=True)
            r.then_inc(q_chain, 1)
            n = t * 6
            wait(dve, q_chain, n + 1)
            dve.tensor_tensor(stats[:, sc:sc + 1], stats[:, lo:lo + 1], stats[:, lo + 1:lo + 2], ALU.max)\
               .then_inc(q_chain, 1)
            wait(dve, q_chain, n + 2)
            dve.tensor_scalar(stats[:, sc:sc + 1], stats[:, sc:sc + 1], EPS, 1.0 / 127.0, ALU.max, ALU.mult)\
               .then_inc(q_chain, 1)
            wait(dve, q_chain, n + 3)
            dve.reciprocal(stats[:, inv:inv + 1], stats[:, sc:sc + 1]).then_inc(q_chain, 1)
            wait(dve, q_chain, n + 4)
            for half in range(2):
                r = dve.tensor_scalar(y_int[:, half * HALF:(half + 1) * HALF], y_ps[p][half][:, :],
                                      stats[:, inv:inv + 1], MAGIC, ALU.mult, ALU.add)
            r.then_inc(y_free, 1)
            wait(dve, y_free, t + 1)
            dve.tensor_scalar(y_int[:, :], y_int[:, :], MAGIC - 128.0, MAGIC + 127.0, ALU.max, ALU.min)\
               .then_inc(q_chain, 1)
            wait(dve, q_chain, n + 5)
            wait(dve, yt_done, t - 1)
            dve.tensor_scalar(y_q[p], y_int[:, :], MAGIC, None, ALU.subtract).then_inc(yq_done, 1)
            dve.tensor_scalar(stats[:, sc:sc + 1], stats[:, sc:sc + 1], alpha[:, 0:1], None, ALU.mult)\
               .then_inc(q_chain, 1)

        def transpose_y(pe, t, p):
            wait(pe, yq_done, t + 1)
            if isinstance(t, int) and t == 0:
                wait(pe, pt_lo_done, STEPS * UNITS)
            else:
                wait(pe, ytq_done, t)
            for k in range(KT):
                mm = pe.transpose(yt_ps[:, k * P:(k + 1) * P], y_q[p][:, k * P:(k + 1) * P], identb[:, :])
            mm.then_inc(yt_done, 1)

        def evac_yt(act, t, p):
            wait(act, yt_done, t + 1)
            wait(act, f_done, t - 1)
            act.activation(yt_q[:, p, :, :].rearrange("p k q -> p (k q)"), yt_ps, ACT.Copy)\
               .then_inc(ytq_done, 1)

        def ternary(pe, t, p):
            wait(pe, ytq_done, t + 1)
            if isinstance(t, int) and t == 0:
                for parity in range(2):
                    wait(pe, o_sum_done[parity], STEPS * NBLK + 1)
                wait(pe, wf_q_done, KT)
            else:
                wait(pe, res_done, t)
            for half in range(2):
                w = slice(half * HALF, (half + 1) * HALF)
                for k in range(KT):
                    mm = pe.matmul(f_ps[half][:, :], yt_q[:, p, k, :], wf_q[:, k, w],
                                   start=(k == 0), stop=(k == KT - 1))
            mm.then_inc(f_done, 1)

        def load_tile(sp, t, p):
            if isinstance(t, int) and t < 2:
                wait(sp, pv_done, STEPS * HG)
            else:
                wait(sp, x_bias_done, t - 1)
            sp.dma_start(x_tile[:, p, :], x[bass.ds(t * P, P), :]).then_inc(x_tile_in[p], 16)

        def add_bias(pool, t, p):
            if isinstance(t, int) and t == 0:
                wait(pool, bias_in, 16)
            wait(pool, x_tile_in[p], (t - p) * 8 + 16)
            wait(pool, res_done, t - 1)
            pool.tensor_tensor(x_bias[:, p, :], x_tile[:, p, :], bias_bc[:, :], ALU.add).then_inc(x_bias_done, 1)

        def finish(dve, t, p):
            wait(dve, f_done, t + 1)
            wait(dve, q_chain, t * 6 + 6)
            wait(dve, x_bias_done, t + 1)
            wait(dve, out_done[p], (t - p) * 8)
            for half in range(2):
                w = slice(half * HALF, (half + 1) * HALF)
                r = dve.scalar_tensor_tensor(out=res[:, p, w], in0=f_ps[half][:, :],
                                             scalar=stats[:, 3 * p + 2:3 * p + 3], in1=x_bias[:, p, w],
                                             op0=ALU.mult, op1=ALU.add)
            r.then_inc(res_done, 1)

        def store(sp, t, p):
            wait(sp, res_done, t + 1)
            sp.dma_start(out[bass.ds(t * P, P), :], res[:, p, :]).then_inc(out_done[p], 16)

        def during_last_step(pe, act, dve, pool, sp):
            for t in range(2):
                sp.add(1.0, load_o, t, t)
            ABS_AT, TERNARY_AT = 1.5, 9.2
            for k in range(KT):
                sp.add(ABS_AT - 1.6 + 0.9 * k if k > 1 else 0.0, load_wf, k)
                act.add(ABS_AT + 0.9 * k, wf_abs, k)
            pool.add(ABS_AT + 0.9 * KT - 0.6, wf_add_partitions)
            dve.add(ABS_AT + 0.9 * KT, wf_scale)
            for k in range(KT):
                if k < 2:
                    sp.add(ABS_AT + 0.9 * (6 + k) + 0.2, load_wf, KT + k)
                elif k < 6:
                    sp.add(TERNARY_AT + 1.3 * (k - 2) + 0.9, load_wf, KT + k)
                if k < 5:
                    dve.add(TERNARY_AT + 1.3 * k, wf_ternary, k)
                if k < 2:
                    sp.add(8.0, load_wo, k)
                if k < 4:
                    sp.add(11.5 + 1.1 * k, load_wo, k + 2)
                    act.add(11.0 + 1.1 * k, wo_high, k)
                    dve.add(11.3 + 1.1 * k, wo_low, k)

        def after_last_step(pe, act, dve, pool, sp):
            for n, k in enumerate(range(4, KT)):
                at = 0.1 + 0.5 * n + 0.9 * (n // 2)
                act.add(at, wo_high, k)
                dve.add(at + 0.3, wo_low, k)
                if k + 2 < KT:
                    sp.add(at + 0.5, load_wo, k + 2)
            for k in range(6, KT):
                sp.add(1.0 + 2 * (k - 6), load_wf, KT + k)
            for k in range(5, KT):
                dve.add(2.9 + 1.8 * (k - 5), wf_ternary, k)
            pool.add(0.0, split_o, 0, 0)
            pool.add(4.0, split_o, 1, 1)
            for k in range(KT):
                pe.add(2.4 + 0.4 * k, attention_out, 0, 0, 0, k)
                pe.add(5.7 + 0.4 * k, attention_out, 0, 0, 1, k)
                pe.add(9.2 + 0.3 * k, attention_out, 1, 1, 0, k)

        def pairs(eng, body):
            with eng.Fori(1, TILES // 2) as i:
                for p in range(2):
                    body(i * 2 + p, p)

        def program(eng, name):
            def emit(**what):
                tables = {n: Timetable() for n in ("pe", "act", "dve", "pool", "sp")}
                step(tables, **what)
                tables[name].run(eng)

            def middle(g):
                with eng.Fori(1, B - 1) as b:
                    it = g * B + b
                    emit(now=(it, g, b), old=(it - 1, g, b - 1), nxt=(it + 1, b + 1))

            emit(now=(0, 0, 0), nxt=(1, 1), first=True)
            middle(0)
            with eng.Fori(1, NG) as g:
                it = g * B
                emit(now=(it - 1, g - 1, B - 1), old=(it - 2, g - 1, B - 2), nxt=(it, 0), qk_for=g)
                emit(now=(it, g, 0), old=(it - 1, g - 1, B - 1), nxt=(it + 1, 1), v_for=g)
                middle(g)
            it, g = STEPS - 1, NG - 1
            emit(now=(it, g, B - 1), old=(it - 1, g, B - 2), more=during_last_step)
            emit(old=(it, g, B - 1), more=after_last_step)

        CONSTS = 4 + 1 + 3 + 3
        block = ctx.enter_context(nc.Block())

        @block.sync
        def _(sp):
            sp.dma_start(cond_bc[:, :], cond.rearrange("b a -> a b").broadcast_to([P, B])).then_inc(cond_in, 16)
            for free in o_sum_done + o_out:
                sp.sem_inc(free, 1)
            program(sp, "sp")
            wait(sp, pv_done, STEPS * HG)
            sp.dma_start(bias_bc[:, :], bias.rearrange("(a n) -> a n", a=1).broadcast_to([P, D])).then_inc(bias_in, 16)
            load_tile(sp, 0, 0)
            load_tile(sp, 1, 1)

            def body(t, p):
                load_o(sp, t, p)
                load_tile(sp, t, p)
                store(sp, t - 2, p)

            for blk in range(NBLK):
                sp.wait_ge(o_out[blk], STEPS * 16 + 1)
            pairs(sp, body)
            for p in range(2):
                store(sp, TILES - 2 + p, p)
            for p in range(2):
                sp.wait_ge(out_done[p], TILES // 2 * 16)

        @block.tensor
        def _(pe):
            wait(pe, const_ready, CONSTS)
            program(pe, "pe")
            transpose_y(pe, 0, 0)
            attention_out_half(pe, 1, 1, 1)
            ternary(pe, 0, 0)

            def body(t, p):
                attention_out_half(pe, t, p, 0)
                transpose_y(pe, t - 1, 1 - p)
                attention_out_half(pe, t, p, 1)
                ternary(pe, t - 1, 1 - p)

            pairs(pe, body)
            transpose_y(pe, TILES - 1, 1)
            ternary(pe, TILES - 1, 1)

        @block.scalar
        def _(act):
            program(act, "act")
            evac_yt(act, 0, 0)
            evac_yt(act, 1, 1)
            pairs(act, lambda t, p: evac_yt(act, t, p))

        @block.vector
        def _(dve):
            for i in range(2):
                dve.memset(pt_hi[i][:, QT - 1, S - 2 * P:S - P].bitcast(F32), 0.0).then_inc(const_ready, 1)
                dve.memset(pt_lo[i][:, QT - 1, S - 2 * P:S - P].bitcast(F32), 0.0).then_inc(const_ready, 1)
            wait(dve, const_ready, CONSTS)
            program(dve, "dve")
            quantise(dve, 0, 0)
            quantise(dve, 1, 1)
            finish(dve, 0, 0)

            def body(t, p):
                quantise(dve, t, p)
                finish(dve, t - 1, 1 - p)

            pairs(dve, body)
            finish(dve, TILES - 1, 1)

        @block.gpsimd
        def _(pool):
            fills = const_ready
            wait(pool, fills, 4)
            pool.memset(one[:, :], 1.0).then_inc(fills, 1)
            for m in (ident, identb, mask):
                pool.memset(m[:, :], 0.0).then_inc(fills, 1)
            wait(pool, fills, 8)
            for m in (ident, identb):
                pool.affine_select(out=m[:, :], in_=m[:, :], compare_op=ALU.not_equal, fill=1.0, base=0,
                                   pattern=[[-1, P]], channel_multiplier=1).then_inc(fills, 1)
            pool.affine_select(out=mask[:, S - P:S], in_=mask[:, S - P:S], compare_op=ALU.is_ge, fill=-MASKED,
                               base=0, pattern=[[-1, P]], channel_multiplier=1).then_inc(fills, 1)
            program(pool, "pool")
            add_bias(pool, 0, 0)
            add_bias(pool, 1, 1)

            def body(t, p):
                split_o(pool, t, p)
                add_bias(pool, t, p)

            pairs(pool, body)


def kernel(x, cond_1, L0_cond_Wq, L0_cond_Wk, L0_cond_Wv, L0_cond_Wo, L0_ffn_weight, L0_ffn_bias):
    import numpy as np
    import concourse.bacc as bacc
    from concourse.bass_utils import run_bass_kernel_spmd

    def grouped(w):
        return np.ascontiguousarray(np.asarray(w).reshape(NG, EG, P, KT).transpose(0, 2, 3, 1))

    def tiled(w):
        return np.ascontiguousarray(np.asarray(w).reshape(D, KT, P).transpose(2, 1, 0))

    arrays = {
        "x": np.ascontiguousarray(x).reshape(B * S, D),
        "xT": np.ascontiguousarray(np.asarray(x).reshape(B, S, P, KT).transpose(0, 2, 3, 1)),
        "cond": np.ascontiguousarray(cond_1),
        "wq": grouped(L0_cond_Wq), "wk": grouped(L0_cond_Wk), "wv": grouped(L0_cond_Wv),
        "wo": tiled(L0_cond_Wo), "wf": tiled(L0_ffn_weight),
        "bias": np.ascontiguousarray(L0_ffn_bias),
    }
    nc = bacc.Bacc("TRN2", target_bir_lowering=False, num_devices=1)
    args = [nc.dram_tensor(n, a.shape, F32, kind="ExternalInput").ap() for n, a in arrays.items()]
    out = nc.dram_tensor("out", (B * S, D), F32, kind="ExternalOutput").ap()
    adaln_ffn_kernel(nc, *args, out)
    r = run_bass_kernel_spmd(nc, [arrays], core_ids=[0])
    return r.results[0]["out"].reshape(B, S, D)
```
